# Optimizing a Trainium2 kernel written in Bass

```python
import numpy as np
import jax
import jax.numpy as jnp

def _softmax(x, axis=-1):
    return jax.nn.softmax(x, axis=axis)

def _gelu(x):
    return jax.nn.gelu(x, approximate=True)

def _silu(x):
    return jax.nn.silu(x)

def _sigmoid(x):
    return jax.nn.sigmoid(x)

def _layernorm(x, axis=-1, eps=1e-05):
    m = jnp.mean(x, axis=axis, keepdims=True)
    v = jnp.var(x, axis=axis, keepdims=True)
    return (x - m) / jnp.sqrt(v + eps)

def _scatter_add(tgt, idx, src, axis=0):
    return tgt.at[idx].add(src)

def _segment_sum(src, seg, n):
    return jax.ops.segment_sum(src, seg, n)
kernel_name = 'mk_dlrm_tower_d1_rec_r8_5437fd'

def setup_inputs(seed: int=0):
    np.random.seed(seed)
    _w = jnp.asarray

    def _rec_inputs():
        import jax
        import jax.numpy as jnp
        _tk = jax.random.key(seed)
        dense_ctx = jax.random.normal(jax.random.fold_in(_tk, 190), (1024, 16), jnp.float32)
        ids = jnp.stack([jax.random.randint(jax.random.fold_in(_tk, 200 + f), (1024,), 0, v, jnp.int32) for f, v in enumerate([1000, 125000, 1000, 1250, 1000, 125000, 1250, 1000, 1250, 1000, 12500, 1000, 12500, 1250, 1250, 1250, 12500, 125000, 1000, 1250, 1000, 12500, 1000, 1000, 12500, 1000, 12500, 1000, 1250, 12500, 1000, 1000])], axis=1)
        tbl_0 = 0.05 * jax.random.normal(jax.random.fold_in(_tk, 500 + 0), (1000, 64), jnp.float32)
        tbl_1 = 0.05 * jax.random.normal(jax.random.fold_in(_tk, 500 + 1), (125000, 64), jnp.float32)
        tbl_2 = 0.05 * jax.random.normal(jax.random.fold_in(_tk, 500 + 2), (1000, 64), jnp.float32)
        tbl_3 = 0.05 * jax.random.normal(jax.random.fold_in(_tk, 500 + 3), (1250, 64), jnp.float32)
        tbl_4 = 0.05 * jax.random.normal(jax.random.fold_in(_tk, 500 + 4), (1000, 64), jnp.float32)
        tbl_5 = 0.05 * jax.random.normal(jax.random.fold_in(_tk, 500 + 5), (125000, 64), jnp.float32)
        tbl_6 = 0.05 * jax.random.normal(jax.random.fold_in(_tk, 500 + 6), (1250, 64), jnp.float32)
        tbl_7 = 0.05 * jax.random.normal(jax.random.fold_in(_tk, 500 + 7), (1000, 64), jnp.float32)
        tbl_8 = 0.05 * jax.random.normal(jax.random.fold_in(_tk, 500 + 8), (1250, 64), jnp.float32)
        tbl_9 = 0.05 * jax.random.normal(jax.random.fold_in(_tk, 500 + 9), (1000, 64), jnp.float32)
        tbl_10 = 0.05 * jax.random.normal(jax.random.fold_in(_tk, 500 + 10), (12500, 64), jnp.float32)
        tbl_11 = 0.05 * jax.random.normal(jax.random.fold_in(_tk, 500 + 11), (1000, 64), jnp.float32)
        tbl_12 = 0.05 * jax.random.normal(jax.random.fold_in(_tk, 500 + 12), (12500, 64), jnp.float32)
        tbl_13 = 0.05 * jax.random.normal(jax.random.fold_in(_tk, 500 + 13), (1250, 64), jnp.float32)
        tbl_14 = 0.05 * jax.random.normal(jax.random.fold_in(_tk, 500 + 14), (1250, 64), jnp.float32)
        tbl_15 = 0.05 * jax.random.normal(jax.random.fold_in(_tk, 500 + 15), (1250, 64), jnp.float32)
        tbl_16 = 0.05 * jax.random.normal(jax.random.fold_in(_tk, 500 + 16), (12500, 64), jnp.float32)
        tbl_17 = 0.05 * jax.random.normal(jax.random.fold_in(_tk, 500 + 17), (125000, 64), jnp.float32)
        tbl_18 = 0.05 * jax.random.normal(jax.random.fold_in(_tk, 500 + 18), (1000, 64), jnp.float32)
        tbl_19 = 0.05 * jax.random.normal(jax.random.fold_in(_tk, 500 + 19), (1250, 64), jnp.float32)
        tbl_20 = 0.05 * jax.random.normal(jax.random.fold_in(_tk, 500 + 20), (1000, 64), jnp.float32)
        tbl_21 = 0.05 * jax.random.normal(jax.random.fold_in(_tk, 500 + 21), (12500, 64), jnp.float32)
        tbl_22 = 0.05 * jax.random.normal(jax.random.fold_in(_tk, 500 + 22), (1000, 64), jnp.float32)
        tbl_23 = 0.05 * jax.random.normal(jax.random.fold_in(_tk, 500 + 23), (1000, 64), jnp.float32)
        tbl_24 = 0.05 * jax.random.normal(jax.random.fold_in(_tk, 500 + 24), (12500, 64), jnp.float32)
        tbl_25 = 0.05 * jax.random.normal(jax.random.fold_in(_tk, 500 + 25), (1000, 64), jnp.float32)
        tbl_26 = 0.05 * jax.random.normal(jax.random.fold_in(_tk, 500 + 26), (12500, 64), jnp.float32)
        tbl_27 = 0.05 * jax.random.normal(jax.random.fold_in(_tk, 500 + 27), (1000, 64), jnp.float32)
        tbl_28 = 0.05 * jax.random.normal(jax.random.fold_in(_tk, 500 + 28), (1250, 64), jnp.float32)
        tbl_29 = 0.05 * jax.random.normal(jax.random.fold_in(_tk, 500 + 29), (12500, 64), jnp.float32)
        tbl_30 = 0.05 * jax.random.normal(jax.random.fold_in(_tk, 500 + 30), (1000, 64), jnp.float32)
        tbl_31 = 0.05 * jax.random.normal(jax.random.fold_in(_tk, 500 + 31), (1000, 64), jnp.float32)
        _rk = jax.random.fold_in(_tk, 7)
        W_top1 = 0.0441942 * jax.random.normal(jax.random.fold_in(_tk, 801), (512, 512), jnp.float32)
        W_top2 = 0.0441942 * jax.random.normal(jax.random.fold_in(_tk, 802), (512, 256), jnp.float32)
        W_top3 = 0.0625 * jax.random.normal(jax.random.fold_in(_tk, 803), (256, 1), jnp.float32)
        b_top1 = jnp.zeros((512,), jnp.float32)
        b_top2 = jnp.zeros((256,), jnp.float32)
        return (dense_ctx, ids, tbl_0, tbl_1, tbl_2, tbl_3, tbl_4, tbl_5, tbl_6, tbl_7, tbl_8, tbl_9, tbl_10, tbl_11, tbl_12, tbl_13, tbl_14, tbl_15, tbl_16, tbl_17, tbl_18, tbl_19, tbl_20, tbl_21, tbl_22, tbl_23, tbl_24, tbl_25, tbl_26, tbl_27, tbl_28, tbl_29, tbl_30, tbl_31, W_top1, b_top1, W_top2, b_top2, W_top3)
    dense_ctx, ids, tbl_0, tbl_1, tbl_2, tbl_3, tbl_4, tbl_5, tbl_6, tbl_7, tbl_8, tbl_9, tbl_10, tbl_11, tbl_12, tbl_13, tbl_14, tbl_15, tbl_16, tbl_17, tbl_18, tbl_19, tbl_20, tbl_21, tbl_22, tbl_23, tbl_24, tbl_25, tbl_26, tbl_27, tbl_28, tbl_29, tbl_30, tbl_31, W_top1, b_top1, W_top2, b_top2, W_top3 = _rec_inputs()

    def _L0_rec_setup():
        import jax, jax.numpy as jnp
        import numpy as np
        BATCH = 256
        NUM_FIELDS = 32
        EMBED = 64
        NPAIRS = NUM_FIELDS * (NUM_FIELDS - 1) // 2
        ROW, COL = np.triu_indices(NUM_FIELDS, k=1)
        ROW = jnp.asarray(ROW)
        COL = jnp.asarray(COL)
        key = jax.random.key(seed)
        k1, k2 = jax.random.split(key)
        emb_inputs = jax.random.normal(k1, (BATCH, NUM_FIELDS, EMBED), dtype=jnp.float32)
        fan_in = NPAIRS * EMBED
        fan_out = EMBED * EMBED
        std = float(np.sqrt(2.0 / (fan_in + fan_out)))
        kernel = jax.random.normal(k2, (EMBED, NPAIRS, EMBED), dtype=jnp.float32) * std
        return {'emb_inputs': emb_inputs, 'kernel': kernel}
    _L0_rec_all = _L0_rec_setup()
    _L0_rec_in = {k: v for k, v in _L0_rec_all.items() if k in ('kernel',)}
    del _L0_rec_all
    return {'dense_ctx': dense_ctx, 'ids': ids, 'tbl_0': tbl_0, 'tbl_1': tbl_1, 'tbl_2': tbl_2, 'tbl_3': tbl_3, 'tbl_4': tbl_4, 'tbl_5': tbl_5, 'tbl_6': tbl_6, 'tbl_7': tbl_7, 'tbl_8': tbl_8, 'tbl_9': tbl_9, 'tbl_10': tbl_10, 'tbl_11': tbl_11, 'tbl_12': tbl_12, 'tbl_13': tbl_13, 'tbl_14': tbl_14, 'tbl_15': tbl_15, 'tbl_16': tbl_16, 'tbl_17': tbl_17, 'tbl_18': tbl_18, 'tbl_19': tbl_19, 'tbl_20': tbl_20, 'tbl_21': tbl_21, 'tbl_22': tbl_22, 'tbl_23': tbl_23, 'tbl_24': tbl_24, 'tbl_25': tbl_25, 'tbl_26': tbl_26, 'tbl_27': tbl_27, 'tbl_28': tbl_28, 'tbl_29': tbl_29, 'tbl_30': tbl_30, 'tbl_31': tbl_31, 'W_top1': W_top1, 'b_top1': b_top1, 'W_top2': W_top2, 'b_top2': b_top2, 'W_top3': W_top3, 'L0_rec_kernel': _L0_rec_in['kernel']}

def reference(dense_ctx, ids, tbl_0, tbl_1, tbl_2, tbl_3, tbl_4, tbl_5, tbl_6, tbl_7, tbl_8, tbl_9, tbl_10, tbl_11, tbl_12, tbl_13, tbl_14, tbl_15, tbl_16, tbl_17, tbl_18, tbl_19, tbl_20, tbl_21, tbl_22, tbl_23, tbl_24, tbl_25, tbl_26, tbl_27, tbl_28, tbl_29, tbl_30, tbl_31, W_top1, b_top1, W_top2, b_top2, W_top3, L0_rec_kernel):
    import jax
    import jax.numpy as jnp

    def _L0_rec_ref(emb_inputs, kernel):
        import jax, jax.numpy as jnp
        import numpy as np
        BATCH = 256
        NUM_FIELDS = 32
        EMBED = 64
        NPAIRS = NUM_FIELDS * (NUM_FIELDS - 1) // 2
        ROW, COL = np.triu_indices(NUM_FIELDS, k=1)
        ROW = jnp.asarray(ROW)
        COL = jnp.asarray(COL)
        p = emb_inputs[:, ROW]
        q = emb_inputs[:, COL]
        kp = jnp.einsum('bpj,ipj->bpi', p, kernel)
        outputs = jnp.sum(kp * q, axis=-1)
        return outputs[:, None, :]
    e = jnp.stack([tbl_0[ids[:, 0]], tbl_1[ids[:, 1]], tbl_2[ids[:, 2]], tbl_3[ids[:, 3]], tbl_4[ids[:, 4]], tbl_5[ids[:, 5]], tbl_6[ids[:, 6]], tbl_7[ids[:, 7]], tbl_8[ids[:, 8]], tbl_9[ids[:, 9]], tbl_10[ids[:, 10]], tbl_11[ids[:, 11]], tbl_12[ids[:, 12]], tbl_13[ids[:, 13]], tbl_14[ids[:, 14]], tbl_15[ids[:, 15]], tbl_16[ids[:, 16]], tbl_17[ids[:, 17]], tbl_18[ids[:, 18]], tbl_19[ids[:, 19]], tbl_20[ids[:, 20]], tbl_21[ids[:, 21]], tbl_22[ids[:, 22]], tbl_23[ids[:, 23]], tbl_24[ids[:, 24]], tbl_25[ids[:, 25]], tbl_26[ids[:, 26]], tbl_27[ids[:, 27]], tbl_28[ids[:, 28]], tbl_29[ids[:, 29]], tbl_30[ids[:, 30]], tbl_31[ids[:, 31]]], axis=1)
    z = _L0_rec_ref(e, L0_rec_kernel)
    z = z.reshape(z.shape[0], -1)
    h = jnp.concatenate([z, dense_ctx], axis=1)
    h = jnp.maximum(h @ W_top1 + b_top1, 0.0)
    h = jnp.maximum(h @ W_top2 + b_top2, 0.0)
    y = h @ W_top3
    return y

_drawn_inputs = setup_inputs


def setup_inputs(seed=0):
    import zlib

    import numpy as np

    out = dict(_drawn_inputs(seed))
    spreads = {'b_top1': (0.0, 0.1), 'b_top2': (0.0, 0.1)}
    factors = {'tbl_0': 8.0,
     'tbl_1': 8.0,
     'tbl_2': 8.0,
     'tbl_3': 8.0,
     'tbl_4': 8.0,
     'tbl_5': 8.0,
     'tbl_6': 8.0,
     'tbl_7': 8.0,
     'tbl_8': 8.0,
     'tbl_9': 8.0,
     'tbl_10': 8.0,
     'tbl_11': 8.0,
     'tbl_12': 8.0,
     'tbl_13': 8.0,
     'tbl_14': 8.0,
     'tbl_15': 8.0,
     'tbl_16': 8.0,
     'tbl_17': 8.0,
     'tbl_18': 8.0,
     'tbl_19': 8.0,
     'tbl_20': 8.0,
     'tbl_21': 8.0,
     'tbl_22': 8.0,
     'tbl_23': 8.0,
     'tbl_24': 8.0,
     'tbl_25': 8.0,
     'tbl_26': 8.0,
     'tbl_27': 8.0,
     'tbl_28': 8.0,
     'tbl_29': 8.0,
     'tbl_30': 8.0,
     'tbl_31': 8.0,
     'L0_rec_kernel': 8.0}
    for name, (base, spread) in spreads.items():
        noise = np.random.default_rng([zlib.crc32(name.encode()), seed]).standard_normal(out[name].shape)
        drawn = base * np.exp(spread * noise) if base else spread * noise
        out[name] = jnp.asarray(drawn.astype(out[name].dtype))
    for name, factor in factors.items():
        out[name] = (out[name] * factor).astype(out[name].dtype)
    return out
```

```python
import concourse.bass as bass
from concourse import mybir
from contextlib import ExitStack

BATCH, FIELDS, EMBED, CTX = 1024, 32, 64, 16
H1, H2 = 512, 256
P = 128
BT = BATCH // P
HALVES = 2
HB = BATCH // HALVES
FIRST = [0] * (FIELDS + 1)
for _c in range(1, FIELDS):
    FIRST[_c + 1] = FIRST[_c] + (_c + 1) // 2
TILES = FIRST[FIELDS]
BANK_TILES = P // 2
BANKS = TILES // BANK_TILES
GROUP = 4
FIELD_OF = [c for c in range(1, FIELDS) for _ in range((c + 1) // 2)]
SPARE = [c for c in range(1, FIELDS, 2)]

CHUNK = 8
CHUNKS = TILES // CHUNK
K_SLOTS, RAW_SLOTS = 4, 2
ROW_SLOTS = 3
MOV_SLOTS = 2
PSUM_SLOTS = 2
PROD_SLOTS = 8

PAIR_AHEAD, SPLIT_AHEAD = 7, 5
GATHER_BOUND = 12


def pair_at(c):
    if c <= GATHER_BOUND:
        return FIRST[c] - 1
    return max(FIRST[c] - PAIR_AHEAD, FIRST[c - 1] + 1) - 1


def split_at(c):
    if c <= GATHER_BOUND:
        return FIRST[c] - 1
    return max(FIRST[c] - SPLIT_AHEAD, FIRST[c - 1] + 1) - 1


def lo_at(c):
    return min(split_at(c) + 1, FIRST[c] - 1)


def chunk_at(k):
    return -1 if k < K_SLOTS else CHUNK * (k - K_SLOTS + 1) + 1


def pairs_until(c):
    return c // 2 + 1


def build(nc, ids, tables, kmat, ctx_t, w1, b1, w2, b2, w3, out):
    f32, f32r, i32 = mybir.dt.float32, mybir.dt.float32r, mybir.dt.int32
    ALU, ACT = mybir.AluOpType, mybir.ActivationFunctionType

    ctx = ExitStack()
    with ctx:
        def sb(name, shape, dt=f32):
            return ctx.enter_context(nc.sbuf_tensor(name, shape, dt))

        def sem(name):
            return ctx.enter_context(nc.semaphore(name))

        idx = sb("idx", [P, BT * FIELDS], i32)
        rows = sb("rows", [P, ROW_SLOTS, BT, 2, EMBED])
        twice = sb("twice", [P, MOV_SLOTS, BT, 2, EMBED])
        k_raw = sb("k_raw", [P, RAW_SLOTS, CHUNK * P])
        k_split = sb("k_split", [P, K_SLOTS, CHUNK * P], f32r)
        mov_hi = sb("mov_hi", [P, MOV_SLOTS, BATCH], f32r)
        mov_lo = sb("mov_lo", [P, MOV_SLOTS, BATCH], f32r)
        pairs = sb("pairs", [P, FIELDS // 2, BATCH])
        prod = sb("prod", [P, PROD_SLOTS, BATCH])
        z = sb("z", [P, BANKS, BATCH])
        ctx_rows = sb("ctx_rows", [P, BANKS, BATCH])
        ident = sb("ident", [P, P])
        pick = sb("pick", [P, 62])
        w1_sb = sb("w1_sb", [P, BANKS, H1])
        w2_sb = sb("w2_sb", [P, H1 // P, H2])
        w3_sb = sb("w3_sb", [P, H2 // P])
        b1_sb = sb("b1_sb", [P, H1 // P])
        b2_sb = sb("b2_sb", [P, H2 // P])
        y_sb = sb("y_sb", [1, BATCH])
        h1 = prod[:, 0:4, :]
        h2 = prod[:, 4:6, :]

        psum = ctx.enter_context(nc.psum_tensor("psum", [P, 8, HB], f32))
        tile_ps = [psum[:, 2 * s:2 * s + 2, :] for s in range(PSUM_SLOTS)]
        turn_ps = psum[:, 4:6, :].rearrange("p h b -> p (h b)")
        z_ps = psum[:, 6:8, :]

        idx_loaded = sem("idx_loaded")
        rows_loaded = [sem(f"rows_loaded{s}") for s in range(2 * ROW_SLOTS)]
        raw_loaded = [sem(f"raw_loaded{s}") for s in range(RAW_SLOTS)]
        weights_loaded = sem("weights_loaded")
        ctx_zeroed = sem("ctx_zeroed")
        ctx_loaded = sem("ctx_loaded")
        ident_blank = sem("ident_blank")
        pick_blank = sem("pick_blank")
        consts_set = sem("consts_set")
        k_hi_done = sem("k_hi_done")
        k_lo_done = sem("k_lo_done")
        doubled = sem("doubled")
        pair_turned = sem("pair_turned")
        field_turned = sem("field_turned")
        pair_done = sem("pair_done")
        mov_hi_done = sem("mov_hi_done")
        mov_lo_done = sem("mov_lo_done")
        tile_done = sem("tile_done")
        prod_done = sem("prod_done")
        summed = sem("summed")
        z_done = sem("z_done")
        h1_ps_done = sem("h1_ps_done")
        h1_done = sem("h1_done")
        h2_ps_done = sem("h2_ps_done")
        h2_done = sem("h2_done")
        y_ps_done = sem("y_ps_done")
        y_done = sem("y_done")
        stored = sem("stored")

        block = ctx.enter_context(nc.Block())

        @block.sync
        def _(sp):
            sp.dma_start(idx[:, :], ids).then_inc(idx_loaded, 16)
            for k in range(CHUNKS):
                if k >= RAW_SLOTS:
                    sp.wait_ge(k_lo_done, k - RAW_SLOTS + 1)
                for half in range(2):
                    sp.dma_start(k_raw[64 * half:64 * half + 64, k % RAW_SLOTS, :],
                                 kmat[:, k * CHUNK * P:(k + 1) * CHUNK * P]).then_inc(raw_loaded[k % RAW_SLOTS], 16)
                if k == 3:
                    for dst, src in ((w1_sb[:, :, :], w1.rearrange("(k p) f -> p k f", p=P)),
                                     (w2_sb[:, :, :], w2.rearrange("(k p) f -> p k f", p=P)),
                                     (w3_sb[:, :], w3), (b1_sb[:, :], b1), (b2_sb[:, :], b2)):
                        sp.dma_start(dst, src).then_inc(weights_loaded, 16)
                    sp.wait_ge(ctx_zeroed, 1)
                    for n, c in enumerate(SPARE):
                        tile = FIRST[c + 1] - 1
                        row = 32 * (tile % GROUP) + 2 * (tile % BANK_TILES // GROUP) + 1
                        sp.dma_start(ctx_rows[row:row + 1, tile // BANK_TILES, :],
                                     ctx_t[n:n + 1, :]).then_inc(ctx_loaded, 16)
            sp.wait_ge(y_done, HALVES)
            sp.dma_start(out.rearrange("b one -> one b"), y_sb[:, :]).then_inc(stored, 16)
            sp.wait_ge(stored, 16)

        @block.gpsimd
        def _(pool):
            nc.gpsimd.memset(ident[:, :], 0.0).then_inc(ident_blank, 1)
            pool.wait_ge(ident_blank, 1)
            nc.gpsimd.affine_select(out=ident[:, :], in_=ident[:, :], compare_op=ALU.not_equal, fill=1.0, base=0,
                                    pattern=[[-1, P]], channel_multiplier=1).then_inc(consts_set, 1)
            pool.wait_ge(idx_loaded, 16)
            for f in range(FIELDS):
                if f >= 2 * ROW_SLOTS:
                    before = f - 2 * ROW_SLOTS
                    pool.wait_ge(pair_turned, pairs_until(before))
                    if before:
                        pool.wait_ge(doubled, before)
                for t in range(BT):
                    nc.gpsimd.indirect_dma_start(
                        out=rows[:, f // 2 % ROW_SLOTS, t, f % 2, :], out_offset=None, in_=tables[f],
                        in_offset=bass.IndirectOffsetOnAxis(ap=idx[:, f * BT + t:f * BT + t + 1], axis=0),
                    ).then_inc(rows_loaded[f % (2 * ROW_SLOTS)], 16)

        @block.tensor
        def _(pe):
            def transpose_pair(c):
                for f in (c - 1, c):
                    pe.wait_ge(rows_loaded[f % (2 * ROW_SLOTS)], 16 * BT * (f // (2 * ROW_SLOTS) + 1))
                if c > 1:
                    pe.wait_ge(mov_lo_done, c - 1)
                for t in range(BT):
                    two_fields = rows[:, c // 2 % ROW_SLOTS, t, :, :].rearrange("p f j -> p (f j)")
                    last = nc.tensor.transpose(turn_ps[:, t * P:(t + 1) * P], two_fields, ident[:, :])
                last.then_inc(pair_turned, 1)

            def transpose_field(c):
                pe.wait_ge(doubled, c)
                if c % 2:
                    pe.wait_ge(pair_done, pairs_until(c))
                else:
                    pe.wait_ge(mov_lo_done, c - 1)
                for t in range(BT):
                    same_field = twice[:, c % MOV_SLOTS, t, :, :].rearrange("p f j -> p (f j)")
                    last = nc.tensor.transpose(turn_ps[:, t * P:(t + 1) * P], same_field, ident[:, :])
                last.then_inc(field_turned, 1)

            def prepare(after):
                for c in range(1, FIELDS):
                    if c % 2 and pair_at(c) == after:
                        transpose_pair(c)
                    if split_at(c) == after:
                        transpose_field(c)

            def sum_group(group, half):
                bank_first = group % (BANK_TILES // GROUP) == 0
                if bank_first:
                    pe.wait_ge(z_done, HALVES * (group // (BANK_TILES // GROUP)))
                t = group % (BANK_TILES // GROUP)
                pe.wait_ge(prod_done, GROUP * (group + 1))
                for g in range(GROUP):
                    last = nc.tensor.matmul(z_ps[32 * g:32 * g + 32, half, :], pick[:, 30 - 2 * t:62 - 2 * t],
                                            prod[:, (GROUP * group + g) % PROD_SLOTS, half * HB:(half + 1) * HB],
                                            start=bank_first, stop=t == BANK_TILES // GROUP - 1)
                last.then_inc(summed, 1)

            pe.wait_ge(consts_set, 3)
            prepare(-1)
            for n in range(TILES):
                c = FIELD_OF[n]
                if n == FIRST[c]:
                    pe.wait_ge(mov_lo_done, c)
                if n % CHUNK == 0:
                    pe.wait_ge(k_lo_done, n // CHUNK + 1)
                if n >= PSUM_SLOTS:
                    pe.wait_ge(prod_done, n - PSUM_SLOTS + 1)
                k_tile = k_split[:, n // CHUNK % K_SLOTS, n % CHUNK * P:(n % CHUNK + 1) * P]
                for half in range(HALVES):
                    b = slice(half * HB, (half + 1) * HB)
                    nc.tensor.matmul(tile_ps[n % PSUM_SLOTS][:, half, :], k_tile, mov_hi[:, c % MOV_SLOTS, b],
                                     start=True, stop=False)
                    last = nc.tensor.matmul(tile_ps[n % PSUM_SLOTS][:, half, :], k_tile, mov_lo[:, c % MOV_SLOTS, b],
                                            start=False, stop=True)
                last.then_inc(tile_done, 1)
                if n % GROUP in (1, 3) and n >= GROUP:
                    sum_group(n // GROUP - 1, n % GROUP // 2)
                prepare(n)
            for half in range(HALVES):
                sum_group(TILES // GROUP - 1, half)

            pe.wait_ge(weights_loaded, 5 * 16)
            pe.wait_ge(z_done, HALVES * BANKS)
            pe.wait_ge(prod_done, TILES)
            for half in range(HALVES):
                b = slice(half * HB, (half + 1) * HB)
                for m in range(H1 // P):
                    for k in range(BANKS):
                        last = nc.tensor.matmul(psum[:, 4 * half + m, :], w1_sb[:, k, m * P:(m + 1) * P], z[:, k, b],
                                                start=k == 0, stop=k == BANKS - 1)
                    last.then_inc(h1_ps_done, 1)
            for half in range(HALVES):
                b = slice(half * HB, (half + 1) * HB)
                pe.wait_ge(h1_done, H1 // P * (half + 1))
                for m in range(H2 // P):
                    for k in range(H1 // P):
                        last = nc.tensor.matmul(psum[:, 4 * half + m, :], w2_sb[:, k, m * P:(m + 1) * P], h1[:, k, b],
                                                start=k == 0, stop=k == H1 // P - 1)
                    last.then_inc(h2_ps_done, 1)
            for half in range(HALVES):
                b = slice(half * HB, (half + 1) * HB)
                pe.wait_ge(h2_done, H2 // P * (half + 1))
                for k in range(H2 // P):
                    last = nc.tensor.matmul(psum[0:1, 4 * half + 2, :], w3_sb[:, k:k + 1], h2[:, k, b],
                                            start=k == 0, stop=k == H2 // P - 1)
                last.then_inc(y_ps_done, 1)

        @block.scalar
        def _(act):
            def round_chunk(k):
                act.wait_ge(raw_loaded[k % RAW_SLOTS], 32 * (k // RAW_SLOTS + 1))
                if k >= K_SLOTS:
                    act.wait_ge(tile_done, CHUNK * (k - K_SLOTS + 1))
                nc.scalar.copy(k_split[:, k % K_SLOTS, :], k_raw[:, k % RAW_SLOTS, :]).then_inc(k_hi_done, 1)

            def double_field(c):
                act.wait_ge(rows_loaded[c % (2 * ROW_SLOTS)], 16 * BT * (c // (2 * ROW_SLOTS) + 1))
                if c > MOV_SLOTS:
                    act.wait_ge(field_turned, c - MOV_SLOTS)
                field = rows[:, c // 2 % ROW_SLOTS, :, c % 2, :]
                nc.scalar.copy(twice[:, c % MOV_SLOTS, :, :, :],
                               field.unsqueeze(2).broadcast_to([P, BT, 2, EMBED])).then_inc(doubled, 1)

            def keep_pair(c):
                act.wait_ge(pair_turned, pairs_until(c))
                nc.scalar.copy(pairs[:, c // 2, :], turn_ps).then_inc(pair_done, 1)

            def round_field(c):
                act.wait_ge(field_turned, c)
                if c > MOV_SLOTS:
                    act.wait_ge(tile_done, FIRST[c - MOV_SLOTS + 1])
                nc.scalar.copy(mov_hi[:, c % MOV_SLOTS, :], turn_ps).then_inc(mov_hi_done, 1)

            for n in range(-1, TILES):
                for k in range(CHUNKS):
                    if chunk_at(k) - 2 == n or (n == -1 and chunk_at(k) == -1):
                        round_chunk(k)
                for c in range(1, FIELDS):
                    if pair_at(c) == n:
                        double_field(c)
                    if c % 2 and pair_at(c) == n:
                        keep_pair(c)
                    if split_at(c) == n:
                        round_field(c)

            for half in range(HALVES):
                b = slice(half * HB, (half + 1) * HB)
                for m in range(H1 // P):
                    act.wait_ge(h1_ps_done, H1 // P * half + m + 1)
                    nc.scalar.activation(h1[:, m, b], psum[:, 4 * half + m, :], ACT.Relu,
                                         bias=b1_sb[:, m:m + 1]).then_inc(h1_done, 1)
            for half in range(HALVES):
                b = slice(half * HB, (half + 1) * HB)
                for m in range(H2 // P):
                    act.wait_ge(h2_ps_done, H2 // P * half + m + 1)
                    nc.scalar.activation(h2[:, m, b], psum[:, 4 * half + m, :], ACT.Relu,
                                         bias=b2_sb[:, m:m + 1]).then_inc(h2_done, 1)
            for half in range(HALVES):
                act.wait_ge(y_ps_done, half + 1)
                nc.scalar.copy(y_sb[:, half * HB:(half + 1) * HB], psum[0:1, 4 * half + 2, :]).then_inc(y_done, 1)

        @block.vector
        def _(dve):
            def finish_chunk(k):
                dve.wait_ge(k_hi_done, k + 1)
                lo = k_split[64:128, k % K_SLOTS, :]
                nc.vector.tensor_tensor(lo, k_raw[64:128, k % RAW_SLOTS, :], lo.bitcast(f32),
                                        ALU.subtract).then_inc(k_lo_done, 1)

            def finish_field(c):
                dve.wait_ge(mov_hi_done, c)
                nc.vector.tensor_tensor(mov_lo[:, c % MOV_SLOTS, :], turn_ps, mov_hi[:, c % MOV_SLOTS, :].bitcast(f32),
                                        ALU.subtract).then_inc(mov_lo_done, 1)

            def read_bank(bank):
                groups = HALVES * BANK_TILES // GROUP * (bank + 1)
                for half in range(HALVES):
                    b = slice(half * HB, (half + 1) * HB)
                    dve.wait_ge(summed, groups - 1 + half)
                    nc.vector.tensor_tensor(z[:, bank, b], z_ps[:, half, :], ctx_rows[:, bank, b],
                                            ALU.add).then_inc(z_done, 1)

            nc.vector.memset(pick[:, :], 0.0).then_inc(pick_blank, 1)
            dve.wait_ge(pick_blank, 1)
            nc.vector.memset(pick[0:64, 30:31], 1.0).then_inc(consts_set, 1)
            nc.vector.memset(pick[64:128, 31:32], 1.0).then_inc(consts_set, 1)
            nc.vector.memset(ctx_rows[:, :, :], 0.0).then_inc(ctx_zeroed, 1)

            for n in range(-1, TILES):
                if n >= 0:
                    c = FIELD_OF[n]
                    k = n - FIRST[c]
                    dve.wait_ge(tile_done, n + 1)
                    if n == FIRST[c] and c % 2:
                        dve.wait_ge(pair_done, pairs_until(c))
                    if n >= PROD_SLOTS:
                        dve.wait_ge(summed, HALVES * ((n - PROD_SLOTS) // GROUP + 1))
                    nc.vector.tensor_tensor(prod[:, n % PROD_SLOTS, :],
                                            tile_ps[n % PSUM_SLOTS].rearrange("p h b -> p (h b)"), pairs[:, k, :],
                                            ALU.mult).then_inc(prod_done, 1)
                for k in range(CHUNKS):
                    if chunk_at(k) == n:
                        finish_chunk(k)
                for c in range(1, FIELDS):
                    if lo_at(c) == n:
                        finish_field(c)
                if n % BANK_TILES == GROUP - 1 and n > GROUP:
                    if n < 2 * BANK_TILES:
                        dve.wait_ge(ctx_loaded, 16 * len(SPARE))
                    read_bank(n // BANK_TILES - 1)
            read_bank(BANKS - 1)


def kernel(ids, dense_ctx, W_top1, b_top1, W_top2, b_top2, W_top3, L0_rec_kernel, **tables):
    import numpy as np
    import concourse.bacc as bacc
    from concourse.bass_utils import run_bass_kernel_spmd

    slots, spare = [], []
    for c in range(1, FIELDS):
        for r in range(c + c % 2):
            if r < c:
                slots.append(r * FIELDS - r * (r + 1) // 2 + c - r - 1)
            else:
                spare.append(len(slots))
                slots.append(-1)
    kept = np.array([s for s, p in enumerate(slots) if p >= 0])
    pair = np.array([p for p in slots if p >= 0])
    K = np.asarray(L0_rec_kernel)
    kmat = np.zeros((EMBED, len(slots), EMBED), K.dtype)
    kmat[:, kept] = K[:, pair]

    tile = np.arange(len(slots)) // 2
    place = P * (tile // BANK_TILES) + 32 * (tile % GROUP) + 2 * (tile % BANK_TILES // GROUP) + np.arange(len(slots)) % 2
    W1 = np.asarray(W_top1)
    w1 = np.zeros_like(W1)
    w1[place[kept]] = W1[pair]
    w1[place[np.array(spare)]] = W1[len(pair):]

    arrays = {
        "ids": np.ascontiguousarray(np.asarray(ids).reshape(BT, P, FIELDS).transpose(1, 2, 0).reshape(P, FIELDS * BT)),
        "kmat": kmat.reshape(EMBED, -1),
        "ctx_t": np.ascontiguousarray(np.asarray(dense_ctx).T),
        "w1": w1,
        "b1": np.ascontiguousarray(np.asarray(b_top1).reshape(-1, P).T),
        "w2": np.ascontiguousarray(np.asarray(W_top2)),
        "b2": np.ascontiguousarray(np.asarray(b_top2).reshape(-1, P).T),
        "w3": np.ascontiguousarray(np.asarray(W_top3).reshape(-1, P).T),
    }
    for f in range(FIELDS):
        arrays[f"tbl_{f}"] = np.ascontiguousarray(np.asarray(tables[f"tbl_{f}"]))

    nc = bacc.Bacc("TRN2", target_bir_lowering=False, num_devices=1)
    ap = {name: nc.dram_tensor(f"{name}_dram", a.shape, mybir.dt.from_np(a.dtype), kind="ExternalInput").ap()
          for name, a in arrays.items()}
    out = nc.dram_tensor("y_dram", (BATCH, 1), mybir.dt.float32, kind="ExternalOutput").ap()
    build(nc, ap["ids"], [ap[f"tbl_{f}"] for f in range(FIELDS)], ap["kmat"], ap["ctx_t"],
          ap["w1"], ap["b1"], ap["w2"], ap["b2"], ap["w3"], out)
    result = run_bass_kernel_spmd(nc, [{f"{name}_dram": a for name, a in arrays.items()}], core_ids=[0])
    return result.results[0]["y_dram"]
```

```python
import concourse.bass as bass
from concourse import mybir
from contextlib import ExitStack

BATCH, FIELDS, EMBED, CTX = 1024, 32, 64, 16
H1, H2 = 512, 256
P = 128
BT = BATCH // P
HALVES = 2
HB = BATCH // HALVES
FIRST = [0] * (FIELDS + 1)
for _c in range(1, FIELDS):
    FIRST[_c + 1] = FIRST[_c] + (_c + 1) // 2
TILES = FIRST[FIELDS]
BANK_TILES = P // 2
BANKS = TILES // BANK_TILES
GROUP = 4
BANK_GROUPS = BANK_TILES // 4
GROUP = 4
GROUPS = TILES // GROUP
SPARE = [c for c in range(1, FIELDS, 2)]
HT = BT // HALVES

C0 = 20
CHUNK = 8
CHUNKS = TILES // CHUNK
K_SLOTS = -(-FIRST[C0] // CHUNK)
RAW_SLOTS = 2
ROW_SLOTS = 6
MOV_SLOTS = 4
PSUM_SLOTS = 6
PROD_SLOTS = 16

STEPS = ([(c, (0,)) for c in range(1, C0)] + [(c, (1,)) for c in range(1, C0)]
         + [(c, (0, 1)) for c in range(C0, FIELDS)])
LOADS = ([(f, (0,)) for f in range(C0)] + [(f, (1,)) for f in range(C0)]
         + [(f, (0, 1)) for f in range(C0, FIELDS)])
LOAD_OF = [LOADS.index(step) for step in STEPS]
UNITS = [(s, n) for s, (c, _) in enumerate(STEPS) for n in range(FIRST[c], FIRST[c + 1])]
UNIT_OF = {(n, h): u for u, (s, n) in enumerate(UNITS) for h in STEPS[s][1]}
FIRST_UNIT = [next(u for u, (s, _) in enumerate(UNITS) if s == step) for step in range(len(STEPS))] + [len(UNITS)]
CHUNK_FIRST = [min(u for u, (_, n) in enumerate(UNITS) if n // CHUNK == k) for k in range(CHUNKS)]
CHUNK_LAST = [max(u for u, (_, n) in enumerate(UNITS) if n // CHUNK == k) for k in range(CHUNKS)]


def ring(uses, size):
    at, taken, owner, place = {}, {}, [None] * size, 0
    for name, width in uses:
        place = -(-place // width) * width % size
        at[name] = place
        taken[name] = sorted({n for n in owner[place:place + width] if n is not None})
        owner[place:place + width] = [name] * width
        place = (place + width) % size
    return at, taken


MOV_AT, MOV_TAKES = ring([(s, len(halves)) for s, (_, halves) in enumerate(STEPS)], MOV_SLOTS)
ROW_AT, ROW_TAKES = ring([(n // 2, len(LOADS[n][1])) for n in range(0, len(LOADS), 2)], ROW_SLOTS)
PROD_AT, PROD_TAKES = ring([(u, len(STEPS[s][1])) for u, (s, _) in enumerate(UNITS)], PROD_SLOTS)


def plan():
    after = [[] for _ in range(len(UNITS) + 8)]

    def put(u, *step):
        after[max(u, 0)].append(step)

    turned = 0
    for s, (c, halves) in enumerate(STEPS):
        first = FIRST_UNIT[s]
        free = max([FIRST_UNIT[n + 1] + 1 for n in MOV_TAKES[s]], default=0)
        waits_for_gather = len(halves) == 1 and c <= (PACED[halves[0]])
        pair_lead, field_lead, lo_lead = (0, 0, 0) if waits_for_gather else LEAD[len(halves)]
        at = max(first - pair_lead, min(free, first), turned)
        put(at, "double", s)
        if c % 2:
            put(at, "pair", s)
        turned = at = max(first - field_lead, min(free, first), at)
        put(at, "field", s)
        put(max(first - lo_lead, at), "lo", s)
    for k in range(CHUNKS):
        at = CHUNK_FIRST[k] - CHUNK_LEAD
        if k >= K_SLOTS:
            at = max(at, CHUNK_LAST[k - K_SLOTS] + 2)
        put(at, "round", k)
        put(max(at + 2, 0) if at > 0 else 0, "finish", k)
    for g in range(GROUPS):
        for h in range(HALVES):
            u = UNIT_OF[GROUP * g + GROUP - 1, h]
            both = len(STEPS[UNITS[u][0]][1]) == 2
            u += SUM_LAG[both][h]
            put(min(u, len(UNITS)), "sum", g, h)
            if g % BANK_GROUPS == BANK_GROUPS - 1:
                put(min(u, len(UNITS)), "read", g // BANK_GROUPS, h)
    order = []
    for u in range(len(after)):
        order += after[u]
        if u < len(UNITS):
            order.append(("tile", u))
    return order


PACED = (6, 6)
SUM_LAG = {False: (5, 5), True: (3, 5)}
LEAD = {1: (12, 9, 8), 2: (8, 6, 6)}
CHUNK_LEAD = 20
ORDER = plan()
NUMBER = {}
for _step in ORDER:
    NUMBER[_step] = sum(1 for k in NUMBER if k[0] == _step[0]) + 1
PSUM_USES = [step for step in ORDER if step[0] in ("tile", "pair", "field")]
PSUM_AT, PSUM_TAKES = ring([(step, len(STEPS[UNITS[step[1]][0] if step[0] == "tile" else step[1]][1]))
                            for step in PSUM_USES], PSUM_SLOTS)
CTX_TILES = [FIRST[c + 1] - 1 for c in SPARE]
assert [k[1] for k in ORDER if k[0] == "field"] == list(range(len(STEPS)))
assert [k[1] for k in ORDER if k[0] == "finish"] == list(range(CHUNKS))


def pairs_until(load):
    return load // 2 + 1


def steps_until(load):
    return sum(1 for n in LOAD_OF if n <= load)


def rows_count(load):
    return 16 * HT * sum(len(LOADS[n][1]) for n in range(load % (2 * ROW_SLOTS), load + 1, 2 * ROW_SLOTS))


def spans(halves):
    return slice(halves[0] * HB, (halves[-1] + 1) * HB)


def build(nc, ids, tables, kmat, ctx_t, w1, b1, w2, b2, w3, out):
    f32, f32r, i32 = mybir.dt.float32, mybir.dt.float32r, mybir.dt.int32
    ALU, ACT = mybir.AluOpType, mybir.ActivationFunctionType

    ctx = ExitStack()
    with ctx:
        def sb(name, shape, dt=f32):
            return ctx.enter_context(nc.sbuf_tensor(name, shape, dt))

        def sem(name):
            return ctx.enter_context(nc.semaphore(name))

        idx = sb("idx", [P, BT * FIELDS], i32)
        rows = sb("rows", [P, ROW_SLOTS * HT, 2, EMBED])
        twice = sb("twice", [P, BT, 2, EMBED])
        k_raw = sb("k_raw", [P, RAW_SLOTS, CHUNK * P])
        k_split = sb("k_split", [P, K_SLOTS, CHUNK * P], f32r)
        mov_hi = sb("mov_hi", [P, MOV_SLOTS * HB], f32r)
        mov_lo = sb("mov_lo", [P, MOV_SLOTS * HB], f32r)
        pairs = sb("pairs", [P, FIELDS // 2, BATCH])
        prod = sb("prod", [P, PROD_SLOTS * HB])
        z = sb("z", [P, BANKS, BATCH])
        ident = sb("ident", [P, P])
        pick = sb("pick", [P, 62])
        w3_sb = sb("w3_sb", [P, H2 // P])
        b1_sb = sb("b1_sb", [P, H1 // P])
        b2_sb = sb("b2_sb", [P, H2 // P])
        w1_sb = k_raw[:, :, :].rearrange("p s (k f) -> p (s k) f", f=H1)
        w2_sb = rows[:, :, :, :].rearrange("p t f j -> p (t f j)")[:, 0:H1 // P * H2].rearrange(
            "p (k f) -> p k f", f=H2)
        layers = prod[:, :].rearrange("p (k b) -> p k b", b=BATCH)
        h1 = layers[:, 0:H1 // P, :]
        h2 = layers[:, H1 // P:(H1 + H2) // P, :]
        y_sb = layers[0:1, (H1 + H2) // P, :]

        psum = ctx.enter_context(nc.psum_tensor("psum", [P, 8, HB], f32))
        z_ps = psum[:, PSUM_SLOTS:PSUM_SLOTS + HALVES, :]

        def slot(step, width):
            return psum[:, PSUM_AT[step]:PSUM_AT[step] + width // HB, :].rearrange("p h b -> p (h b)")

        idx_loaded = sem("idx_loaded")
        rows_loaded = [sem(f"rows_loaded{s}") for s in range(2 * ROW_SLOTS)]
        raw_loaded = [sem(f"raw_loaded{s}") for s in range(RAW_SLOTS)]
        small_loaded = sem("small_loaded")
        w1_loaded = sem("w1_loaded")
        w2_loaded = sem("w2_loaded")
        ctx_loaded = sem("ctx_loaded")
        last_ctx_loaded = sem("last_ctx_loaded")
        ident_blank = sem("ident_blank")
        pick_blank = sem("pick_blank")
        consts_set = sem("consts_set")
        k_hi_done = sem("k_hi_done")
        k_lo_done = sem("k_lo_done")
        doubled = sem("doubled")
        pair_turned = sem("pair_turned")
        field_turned = sem("field_turned")
        pair_done = sem("pair_done")
        mov_hi_done = sem("mov_hi_done")
        mov_lo_done = sem("mov_lo_done")
        tile_done = sem("tile_done")
        prod_done = sem("prod_done")
        summed = sem("summed")
        z_done = sem("z_done")
        h1_ps_done = sem("h1_ps_done")
        h1_done = sem("h1_done")
        h2_ps_done = sem("h2_ps_done")
        h2_done = sem("h2_done")
        y_ps_done = sem("y_ps_done")
        y_done = sem("y_done")
        stored = sem("stored")

        block = ctx.enter_context(nc.Block())

        @block.sync
        def _(sp):
            def load_chunk(k):
                for half in range(2):
                    sp.dma_start(k_raw[64 * half:64 * half + 64, k % RAW_SLOTS, :],
                                 kmat[:, k * CHUNK * P:(k + 1) * CHUNK * P]).then_inc(raw_loaded[k % RAW_SLOTS], 16)

            sp.dma_start(idx[:, :], ids).then_inc(idx_loaded, 16)
            for k in range(RAW_SLOTS):
                load_chunk(k)
            for dst, src in ((w3_sb[:, :], w3), (b1_sb[:, :], b1), (b2_sb[:, :], b2)):
                sp.dma_start(dst, src).then_inc(small_loaded, 16)
            for step in ORDER:
                if step[0] == "finish" and step[1] + RAW_SLOTS < CHUNKS:
                    sp.wait_ge(k_lo_done, step[1] + 1)
                    load_chunk(step[1] + RAW_SLOTS)
                if step[0] == "read":
                    bank, h = step[1:]
                    sp.wait_ge(z_done, NUMBER[step])
                    for n, tile in enumerate(CTX_TILES):
                        if tile // BANK_TILES == bank:
                            row = 32 * (tile % GROUP) + 2 * (tile % BANK_TILES // GROUP) + 1
                            sp.dma_start(z[row:row + 1, bank, spans((h,))], ctx_t[n:n + 1, spans((h,))]).then_inc(
                                last_ctx_loaded if bank == BANKS - 1 else ctx_loaded, 16)
                if step == ("finish", CHUNKS - 1):
                    sp.wait_ge(k_lo_done, CHUNKS)
                    sp.dma_start(w1_sb, w1.rearrange("(k p) f -> p k f", p=P)).then_inc(w1_loaded, 16)
                if step == ("field", len(STEPS) - 1):
                    sp.wait_ge(pair_turned, pairs_until(len(LOADS) - 1))
                    sp.wait_ge(doubled, len(STEPS))
                    sp.dma_start(w2_sb, w2.rearrange("(k p) f -> p k f", p=P)).then_inc(w2_loaded, 16)
            sp.wait_ge(y_done, HALVES)
            sp.dma_start(out.rearrange("b one -> one b"), y_sb).then_inc(stored, 16)
            sp.wait_ge(stored, 16)

        @block.gpsimd
        def _(pool):
            def gather(load):
                f, halves = LOADS[load]
                for old in ROW_TAKES[load // 2]:
                    pool.wait_ge(pair_turned, old + 1)
                    pool.wait_ge(doubled, steps_until(2 * old + 1))
                for n, t in enumerate(range(halves[0] * HT, (halves[-1] + 1) * HT)):
                    nc.gpsimd.indirect_dma_start(
                        out=rows[:, ROW_AT[load // 2] * HT + n, load % 2, :], out_offset=None, in_=tables[f],
                        in_offset=bass.IndirectOffsetOnAxis(ap=idx[:, f * BT + t:f * BT + t + 1], axis=0),
                    ).then_inc(rows_loaded[load % (2 * ROW_SLOTS)], 16)

            pool.wait_ge(idx_loaded, 16)
            gather(0)
            gather(1)
            nc.gpsimd.memset(ident[:, :], 0.0).then_inc(ident_blank, 1)
            pool.wait_ge(ident_blank, 1)
            nc.gpsimd.affine_select(out=ident[:, :], in_=ident[:, :], compare_op=ALU.not_equal, fill=1.0, base=0,
                                    pattern=[[-1, P]], channel_multiplier=1).then_inc(consts_set, 1)
            for load in range(2, len(LOADS)):
                gather(load)

        @block.tensor
        def _(pe):
            def wait_slot(step):
                for old in PSUM_TAKES[step]:
                    done = {"tile": prod_done, "pair": pair_done, "field": mov_lo_done}[old[0]]
                    pe.wait_ge(done, NUMBER[old])

            def transpose_pair(step):
                load, halves = LOAD_OF[step[1]], STEPS[step[1]][1]
                for n in (load - 1, load):
                    pe.wait_ge(rows_loaded[n % (2 * ROW_SLOTS)], rows_count(n))
                wait_slot(step)
                width = HB * len(halves)
                for n in range(HT * len(halves)):
                    two_fields = rows[:, ROW_AT[load // 2] * HT + n, :, :].rearrange("p f j -> p (f j)")
                    last = nc.tensor.transpose(slot(step, width)[:, n * P:(n + 1) * P], two_fields, ident[:, :])
                last.then_inc(pair_turned, 1)

            def transpose_field(step):
                pe.wait_ge(doubled, step[1] + 1)
                wait_slot(step)
                width = HB * len(STEPS[step[1]][1])
                for n in range(HT * len(STEPS[step[1]][1])):
                    same_field = twice[:, n, :, :].rearrange("p f j -> p (f j)")
                    last = nc.tensor.transpose(slot(step, width)[:, n * P:(n + 1) * P], same_field, ident[:, :])
                last.then_inc(field_turned, 1)

            def make_tile(step):
                u = step[1]
                s, tile = UNITS[u]
                halves = STEPS[s][1]
                if u == FIRST_UNIT[s]:
                    pe.wait_ge(mov_lo_done, s + 1)
                if u == CHUNK_FIRST[tile // CHUNK]:
                    pe.wait_ge(k_lo_done, tile // CHUNK + 1)
                wait_slot(step)
                k_tile = k_split[:, tile // CHUNK % K_SLOTS, tile % CHUNK * P:(tile % CHUNK + 1) * P]
                for n in range(len(halves)):
                    bank = psum[:, PSUM_AT[step] + n, :]
                    b = slice((MOV_AT[s] + n) * HB, (MOV_AT[s] + n + 1) * HB)
                    nc.tensor.matmul(bank, k_tile, mov_hi[:, b], start=True, stop=False)
                    last = nc.tensor.matmul(bank, k_tile, mov_lo[:, b], start=False, stop=True)
                last.then_inc(tile_done, 1)

            def sum_group(step):
                group, h = step[1:]
                t = group % BANK_GROUPS
                if t == 0 and group:
                    pe.wait_ge(z_done, NUMBER["read", group // BANK_GROUPS - 1, h])
                units = [UNIT_OF[GROUP * group + g, h] for g in range(GROUP)]
                pe.wait_ge(prod_done, units[-1] + 1)
                for g, u in enumerate(units):
                    n = STEPS[UNITS[u][0]][1].index(h)
                    last = nc.tensor.matmul(z_ps[32 * g:32 * g + 32, h, :], pick[:, 30 - 2 * t:62 - 2 * t],
                                            prod[:, (PROD_AT[u] + n) * HB:(PROD_AT[u] + n + 1) * HB],
                                            start=t == 0, stop=t == BANK_GROUPS - 1)
                last.then_inc(summed, 1)

            pe.wait_ge(consts_set, 3)
            for step in ORDER:
                if step[0] == "pair":
                    transpose_pair(step)
                if step[0] == "field":
                    transpose_field(step)
                if step[0] == "tile":
                    make_tile(step)
                if step[0] == "sum":
                    sum_group(step)

            def layer1(half, m, k):
                return nc.tensor.matmul(psum[:, 4 * half + m, :], w1_sb[:, k, m * P:(m + 1) * P],
                                        z[:, k, spans((half,))], start=k == 0, stop=k == BANKS - 1)

            pe.wait_ge(w1_loaded, 16)
            pe.wait_ge(prod_done, len(UNITS))
            pe.wait_ge(ctx_loaded, 16 * HALVES * sum(t // BANK_TILES < BANKS - 1 for t in CTX_TILES))
            for m in range(H1 // P):
                for k in range(BANKS - 1):
                    layer1(0, m, k)
            pe.wait_ge(last_ctx_loaded, 16 * HALVES * sum(t // BANK_TILES == BANKS - 1 for t in CTX_TILES))
            for m in range(H1 // P):
                layer1(0, m, BANKS - 1).then_inc(h1_ps_done, 1)
            for m in range(H1 // P):
                for k in range(BANKS):
                    last = layer1(1, m, k)
                last.then_inc(h1_ps_done, 1)
            pe.wait_ge(w2_loaded, 16)
            pe.wait_ge(small_loaded, 3 * 16)
            for half in range(HALVES):
                pe.wait_ge(h1_done, H1 // P * (half + 1))
                for m in range(H2 // P):
                    for k in range(H1 // P):
                        last = nc.tensor.matmul(psum[:, 4 * half + m, :], w2_sb[:, k, m * P:(m + 1) * P],
                                                h1[:, k, spans((half,))], start=k == 0, stop=k == H1 // P - 1)
                    last.then_inc(h2_ps_done, 1)
            for half in range(HALVES):
                pe.wait_ge(h2_done, H2 // P * (half + 1))
                for k in range(H2 // P):
                    last = nc.tensor.matmul(psum[0:1, 4 * half + 2, :], w3_sb[:, k:k + 1], h2[:, k, spans((half,))],
                                            start=k == 0, stop=k == H2 // P - 1)
                last.then_inc(y_ps_done, 1)

        @block.scalar
        def _(act):
            def round_chunk(k):
                act.wait_ge(raw_loaded[k % RAW_SLOTS], 32 * (k // RAW_SLOTS + 1))
                if k >= K_SLOTS:
                    act.wait_ge(tile_done, CHUNK_LAST[k - K_SLOTS] + 1)
                nc.scalar.copy(k_split[:, k % K_SLOTS, :], k_raw[:, k % RAW_SLOTS, :]).then_inc(k_hi_done, 1)

            def double_field(s):
                load, halves = LOAD_OF[s], STEPS[s][1]
                act.wait_ge(rows_loaded[load % (2 * ROW_SLOTS)], rows_count(load))
                if s:
                    act.wait_ge(field_turned, s)
                tiles = HT * len(halves)
                first = ROW_AT[load // 2] * HT
                field = rows[:, first:first + tiles, load % 2, :]
                nc.scalar.copy(twice[:, 0:tiles, :, :],
                               field.unsqueeze(2).broadcast_to([P, tiles, 2, EMBED])).then_inc(doubled, 1)

            def keep_pair(step):
                c, halves = STEPS[step[1]]
                act.wait_ge(pair_turned, NUMBER[step])
                nc.scalar.copy(pairs[:, c // 2, spans(halves)], slot(step, HB * len(halves))).then_inc(pair_done, 1)

            def round_field(step):
                s = step[1]
                act.wait_ge(field_turned, s + 1)
                if MOV_TAKES[s]:
                    act.wait_ge(tile_done, FIRST_UNIT[MOV_TAKES[s][-1] + 1])
                width = HB * len(STEPS[s][1])
                nc.scalar.copy(mov_hi[:, MOV_AT[s] * HB:MOV_AT[s] * HB + width], slot(step, width)).then_inc(mov_hi_done, 1)

            def read_bank(step):
                bank, h = step[1:]
                act.wait_ge(summed, NUMBER["sum", BANK_GROUPS * (bank + 1) - 1, h])
                nc.scalar.copy(z[:, bank, spans((h,))], z_ps[:, h, :]).then_inc(z_done, 1)

            for step in ORDER:
                if step[0] == "round":
                    round_chunk(step[1])
                if step[0] == "double":
                    double_field(step[1])
                if step[0] == "pair":
                    keep_pair(step)
                if step[0] == "field":
                    round_field(step)
                if step[0] == "read":
                    read_bank(step)

            act.wait_ge(small_loaded, 3 * 16)
            for half in range(HALVES):
                for m in range(H1 // P):
                    act.wait_ge(h1_ps_done, H1 // P * half + m + 1)
                    nc.scalar.activation(h1[:, m, spans((half,))], psum[:, 4 * half + m, :], ACT.Relu,
                                         bias=b1_sb[:, m:m + 1]).then_inc(h1_done, 1)
            for half in range(HALVES):
                for m in range(H2 // P):
                    act.wait_ge(h2_ps_done, H2 // P * half + m + 1)
                    nc.scalar.activation(h2[:, m, spans((half,))], psum[:, 4 * half + m, :], ACT.Relu,
                                         bias=b2_sb[:, m:m + 1]).then_inc(h2_done, 1)
            for half in range(HALVES):
                act.wait_ge(y_ps_done, half + 1)
                nc.scalar.copy(y_sb[:, spans((half,))], psum[0:1, 4 * half + 2, :]).then_inc(y_done, 1)

        @block.vector
        def _(dve):
            def finish_chunk(k):
                dve.wait_ge(k_hi_done, k + 1)
                lo = k_split[64:128, k % K_SLOTS, :]
                nc.vector.tensor_tensor(lo, k_raw[64:128, k % RAW_SLOTS, :], lo.bitcast(f32),
                                        ALU.subtract).then_inc(k_lo_done, 1)

            def finish_field(s):
                dve.wait_ge(mov_hi_done, s + 1)
                width = HB * len(STEPS[s][1])
                b = slice(MOV_AT[s] * HB, MOV_AT[s] * HB + width)
                nc.vector.tensor_tensor(mov_lo[:, b], slot(("field", s), width), mov_hi[:, b].bitcast(f32),
                                        ALU.subtract).then_inc(mov_lo_done, 1)

            def multiply(step):
                u = step[1]
                s, tile = UNITS[u]
                c, halves = STEPS[s]
                dve.wait_ge(tile_done, u + 1)
                if u == FIRST_UNIT[s] and c % 2:
                    dve.wait_ge(pair_done, NUMBER["pair", s])
                if PROD_TAKES[u]:
                    old_step, old_tile = UNITS[PROD_TAKES[u][-1]]
                    dve.wait_ge(summed, NUMBER["sum", old_tile // GROUP, STEPS[old_step][1][-1]])
                width = HB * len(halves)
                nc.vector.tensor_tensor(prod[:, PROD_AT[u] * HB:PROD_AT[u] * HB + width], slot(step, width),
                                        pairs[:, tile - FIRST[c], spans(halves)], ALU.mult).then_inc(prod_done, 1)

            nc.vector.memset(pick[:, :], 0.0).then_inc(pick_blank, 1)
            dve.wait_ge(pick_blank, 1)
            nc.vector.memset(pick[0:64, 30:31], 1.0).then_inc(consts_set, 1)
            nc.vector.memset(pick[64:128, 31:32], 1.0).then_inc(consts_set, 1)
            for step in ORDER:
                if step[0] == "finish":
                    finish_chunk(step[1])
                if step[0] == "lo":
                    finish_field(step[1])
                if step[0] == "tile":
                    multiply(step)


def kernel(ids, dense_ctx, W_top1, b_top1, W_top2, b_top2, W_top3, L0_rec_kernel, **tables):
    import numpy as np
    import concourse.bacc as bacc
    from concourse.bass_utils import run_bass_kernel_spmd

    slots, spare = [], []
    for c in range(1, FIELDS):
        for r in range(c + c % 2):
            if r < c:
                slots.append(r * FIELDS - r * (r + 1) // 2 + c - r - 1)
            else:
                spare.append(len(slots))
                slots.append(-1)
    kept = np.array([s for s, p in enumerate(slots) if p >= 0])
    pair = np.array([p for p in slots if p >= 0])
    K = np.asarray(L0_rec_kernel)
    kmat = np.zeros((EMBED, len(slots), EMBED), K.dtype)
    kmat[:, kept] = K[:, pair]

    tile = np.arange(len(slots)) // 2
    place = P * (tile // BANK_TILES) + 32 * (tile % GROUP) + 2 * (tile % BANK_TILES // GROUP) + np.arange(len(slots)) % 2
    W1 = np.asarray(W_top1)
    w1 = np.zeros_like(W1)
    w1[place[kept]] = W1[pair]
    w1[place[np.array(spare)]] = W1[len(pair):]

    arrays = {
        "ids": np.ascontiguousarray(np.asarray(ids).reshape(BT, P, FIELDS).transpose(1, 2, 0).reshape(P, FIELDS * BT)),
        "kmat": kmat.reshape(EMBED, -1),
        "ctx_t": np.ascontiguousarray(np.asarray(dense_ctx).T),
        "w1": w1,
        "b1": np.ascontiguousarray(np.asarray(b_top1).reshape(-1, P).T),
        "w2": np.ascontiguousarray(np.asarray(W_top2)),
        "b2": np.ascontiguousarray(np.asarray(b_top2).reshape(-1, P).T),
        "w3": np.ascontiguousarray(np.asarray(W_top3).reshape(-1, P).T),
    }
    for f in range(FIELDS):
        arrays[f"tbl_{f}"] = np.ascontiguousarray(np.asarray(tables[f"tbl_{f}"]))

    nc = bacc.Bacc("TRN2", target_bir_lowering=False, num_devices=1)
    ap = {name: nc.dram_tensor(f"{name}_dram", a.shape, mybir.dt.from_np(a.dtype), kind="ExternalInput").ap()
          for name, a in arrays.items()}
    out = nc.dram_tensor("y_dram", (BATCH, 1), mybir.dt.float32, kind="ExternalOutput").ap()
    build(nc, ap["ids"], [ap[f"tbl_{f}"] for f in range(FIELDS)], ap["kmat"], ap["ctx_t"],
          ap["w1"], ap["b1"], ap["w2"], ap["b2"], ap["w3"], out)
    result = run_bass_kernel_spmd(nc, [{f"{name}_dram": a for name, a in arrays.items()}], core_ids=[0])
    return result.results[0]["y_dram"]
```

```python
import concourse.bass as bass
from concourse import mybir
from contextlib import ExitStack

BATCH, FIELDS, EMBED = 1024, 32, 64
H1, H2 = 512, 256
P = 128
BT = BATCH // P
HALVES = 2
HB = BATCH // HALVES
FIRST = [0] * (FIELDS + 1)
for _c in range(1, FIELDS):
    FIRST[_c + 1] = FIRST[_c] + (_c + 1) // 2
TILES = FIRST[FIELDS]
BANK_TILES = P // 2
BANKS = TILES // BANK_TILES
GROUP = 4
BANK_GROUPS = BANK_TILES // GROUP
GROUPS = TILES // GROUP
SPARE = [c for c in range(1, FIELDS, 2)]
HT = BT // HALVES

C0 = 24
CHUNK = 8
CHUNKS = TILES // CHUNK
K_SLOTS = -(-FIRST[C0] // CHUNK)
CHUNK_COLS = CHUNK * P // 2
LATE_PAIRS = list(range(C0 // 2, FIELDS // 2))
LATE_BANKS = [b for b in range(BANKS) if (b + 1) * BANK_TILES > FIRST[C0]]
LENT = len(LATE_PAIRS) + len(LATE_BANKS)
OWN_SLOTS = K_SLOTS - LENT
RAW_SLOTS = 4
ROW_SLOTS = 4
MOV_SLOTS = 4
PSUM_SLOTS = 6
PROD_SLOTS = 16

BLENDED = 2
BLEND_AT = 10
assert FIRST[2 * BLENDED] % GROUP == 0 and FIRST[2 * BLEND_AT] % GROUP == 0 and FIRST[C0] % GROUP == 0
FIELD_PAIRS = [(k, (0,)) for k in range(BLEND_AT)] + [(k, (1,)) for k in range(BLENDED)]
FIELD_PAIRS += [(k, (0,)) for k in range(BLEND_AT, C0 // 2)]
FIELD_PAIRS += [(k, (1,)) for k in range(BLENDED, C0 // 2)] + [(k, (0, 1)) for k in range(C0 // 2, FIELDS // 2)]
STEPS = [(c, halves) for k, halves in FIELD_PAIRS for c in (2 * k, 2 * k + 1) if c]
LOADS = [(f, halves) for k, halves in FIELD_PAIRS for f in (2 * k, 2 * k + 1)]
LOAD_OF = [LOADS.index(step) for step in STEPS]
UNITS = []
for _s, (_c, _halves) in enumerate(STEPS):
    _parts = [(n, h) for n in range(FIRST[_c], FIRST[_c + 1]) for h in _halves]
    UNITS += [(_s, _parts[i:i + 2]) for i in range(0, len(_parts), 2)]
UNIT_OF = {part: u for u, (_, parts) in enumerate(UNITS) for part in parts}
FIRST_UNIT = [next(u for u, (s, _) in enumerate(UNITS) if s == step) for step in range(len(STEPS))] + [len(UNITS)]
CHUNK_FIRST = [min(UNIT_OF[part] for part in UNIT_OF if part[0] // CHUNK == k) for k in range(CHUNKS)]
CHUNK_LAST = [max(UNIT_OF[part] for part in UNIT_OF if part[0] // CHUNK == k) for k in range(CHUNKS)]


def ring(uses, size):
    at, taken, owner, place = {}, {}, [None] * size, 0
    for name, width in uses:
        place = -(-place // width) * width % size
        at[name] = place
        taken[name] = sorted({n for n in owner[place:place + width] if n is not None})
        owner[place:place + width] = [name] * width
        place = (place + width) % size
    return at, taken


PAIR_OF = [s if c == 1 or c % 2 == 0 else s - 1 for s, (c, _) in enumerate(STEPS)]
MOV_AT, MOV_TAKES = ring([(s, len(halves)) for s, (_, halves) in enumerate(STEPS)], MOV_SLOTS)
ROW_AT, ROW_TAKES = ring([(n // 2, len(LOADS[n][1])) for n in range(0, len(LOADS), 2)], ROW_SLOTS)
PROD_AT, PROD_TAKES = ring([(u, len(parts)) for u, (_, parts) in enumerate(UNITS)], PROD_SLOTS)


def plan():
    after = [[] for _ in range(len(UNITS) + 8)]

    def put(u, *step):
        after[max(u, 0)].append(step)

    pair_at = field_at = lo_at = copy_at = 0
    for s, (c, halves) in enumerate(STEPS):
        first = FIRST_UNIT[s]
        free = max([FIRST_UNIT[n + 1] + 1 for n in MOV_TAKES[s]], default=0)
        lead = LEAD[halves][min(c // 2, len(LEAD[halves]) - 1)]
        pair_lead, lo_lead, field_lead, copy_lead = [max(lead - n, 0) for n in LATER]
        if PAIR_OF[s] == s:
            pair_at = max(first - pair_lead, pair_at)
            put(pair_at, "pair", s)
            lo_at = max(first - lo_lead, pair_at, copy_at)
            put(lo_at, "lo", s)
        field_at = max(first - field_lead, min(free, first), field_at, pair_at)
        copy_at = max(first - copy_lead, field_at, lo_at)
        put(field_at, "field", s)
        put(copy_at, "copy", s)
    for k in range(CHUNKS):
        at = CHUNK_FIRST[k] - CHUNK_LEAD[k >= K_SLOTS]
        if k >= K_SLOTS:
            at = max(at, CHUNK_LAST[k - OWN_SLOTS] + 2)
        put(at, "round", k)
        put(at + 1 if at > 0 else 0, "finish", k)
        put(at + 2 if at > 0 else 0, "spread", k)
    for g in range(GROUPS):
        for h in range(HALVES):
            at = min(UNIT_OF[GROUP * g + GROUP - 1, h] + SUM_LAG, len(UNITS))
            put(at, "sum", g, h)
            if g % BANK_GROUPS == BANK_GROUPS - 1:
                put(at, "read", g // BANK_GROUPS, h)
    order = []
    for u in range(len(after)):
        order += after[u]
        if u < len(UNITS):
            order.append(("tile", u))
    return order


SUM_LAG = 5
LEAD = {(0,): [0, 0, 1, 1, 4, 4, 4], (1,): [7, 5, 9, 6, 7], (0, 1): [6]}
LATER = (0, 1, 1, 3)
CHUNK_LEAD = (14, 22)
ORDER = plan()
NUMBER = {}
for _step in ORDER:
    NUMBER[_step] = sum(1 for k in NUMBER if k[0] == _step[0]) + 1
PSUM_USES = [step for step in ORDER if step[0] in ("tile", "pair")]
PSUM_AT, PSUM_TAKES = ring([(step, len(UNITS[step[1]][1] if step[0] == "tile" else STEPS[step[1]][1]))
                            for step in PSUM_USES], PSUM_SLOTS)
CTX_TILES = [FIRST[c + 1] - 1 for c in SPARE]
assert [k[1] for k in ORDER if k[0] == "field"] == list(range(len(STEPS)))
assert [k[1] for k in ORDER if k[0] == "spread"] == list(range(CHUNKS))


def rows_count(load):
    return 16 * HT * sum(len(LOADS[n][1]) for n in range(load % (2 * ROW_SLOTS), load + 1, 2 * ROW_SLOTS))


def own(c):
    return slice(64 * (c % 2), 64 * (c % 2) + 64)


def spans(halves):
    return slice(halves[0] * HB, (halves[-1] + 1) * HB)


def build(nc, ids, tables, kmat, ctx_t, w1, b1, w2, b2, w3, out):
    f32, f32r, i32 = mybir.dt.float32, mybir.dt.float32r, mybir.dt.int32
    ALU, ACT = mybir.AluOpType, mybir.ActivationFunctionType

    ctx = ExitStack()
    with ctx:
        def sb(name, shape, dt=f32):
            return ctx.enter_context(nc.sbuf_tensor(name, shape, dt))

        def sem(name):
            return ctx.enter_context(nc.semaphore(name))

        with nc.sbuf_tensor("k_lent", [P, LENT, CHUNK * P], f32r) as k_lent:
            pass
        late_pairs = sb("late_pairs", [P, len(LATE_PAIRS), BATCH])
        late_z = sb("late_z", [P, len(LATE_BANKS), BATCH])
        idx = sb("idx", [P, BT * FIELDS], i32)
        rows = sb("rows", [P, ROW_SLOTS * HT, 2, EMBED])
        k_raw = sb("k_raw", [P, RAW_SLOTS, CHUNK_COLS])
        k_hi = sb("k_hi", [P, 2, CHUNK_COLS], f32r)
        k_lo = sb("k_lo", [P, 2, CHUNK_COLS], f32r)
        pair_lo = sb("pair_lo", [P, BATCH])
        k_own = sb("k_own", [P, OWN_SLOTS, CHUNK * P], f32r)
        mov_hi = sb("mov_hi", [P, MOV_SLOTS * HB], f32r)
        mov_lo = sb("mov_lo", [P, MOV_SLOTS * HB], f32r)
        early_pairs = sb("early_pairs", [P, LATE_PAIRS[0], BATCH])
        prod = sb("prod", [P, PROD_SLOTS * HB])
        early_z = sb("early_z", [P, LATE_BANKS[0], BATCH])
        ident = sb("ident", [P, P])
        pick = sb("pick", [P, 62])
        w3_sb = sb("w3_sb", [P, H2 // P])
        b1_sb = sb("b1_sb", [P, H1 // P])
        b2_sb = sb("b2_sb", [P, H2 // P])
        w1_sb = k_raw[:, :, :].rearrange("p s c -> p (s c)")[:, 0:BANKS * H1].rearrange("p (k f) -> p k f", f=H1)
        w2_sb = rows[:, :, :, :].rearrange("p t f j -> p (t f j)")[:, 0:H1 // P * H2].rearrange(
            "p (k f) -> p k f", f=H2)
        layers = prod[:, :].rearrange("p (k b) -> p k b", b=BATCH)
        h1 = layers[:, 0:H1 // P, :]
        h2 = layers[:, H1 // P:(H1 + H2) // P, :]
        y_sb = layers[0:1, (H1 + H2) // P, :]

        psum = ctx.enter_context(nc.psum_tensor("psum", [P, 8, HB], f32))
        z_ps = psum[:, PSUM_SLOTS:PSUM_SLOTS + HALVES, :]

        def k_slot(k):
            return k_lent[:, k, :] if k < LENT else k_own[:, (k - LENT) % OWN_SLOTS, :]

        def pair(k, halves):
            place = early_pairs[:, k, :] if k < LATE_PAIRS[0] else late_pairs[:, k - LATE_PAIRS[0], :]
            return place[:, spans(halves)]

        def z_bank(bank, half):
            place = early_z[:, bank, :] if bank < LATE_BANKS[0] else late_z[:, bank - LATE_BANKS[0], :]
            return place[:, spans((half,))]

        def slot(step, width):
            return psum[:, PSUM_AT[step]:PSUM_AT[step] + width // HB, :].rearrange("p h b -> p (h b)")

        idx_loaded = sem("idx_loaded")
        rows_loaded = [sem(f"rows_loaded{s}") for s in range(2 * ROW_SLOTS)]
        raw_loaded = [sem(f"raw_loaded{s}") for s in range(RAW_SLOTS)]
        small_loaded = sem("small_loaded")
        w1_loaded = sem("w1_loaded")
        w2_loaded = sem("w2_loaded")
        ctx_loaded = sem("ctx_loaded")
        last_ctx_loaded = sem("last_ctx_loaded")
        ident_blank = sem("ident_blank")
        pick_blank = sem("pick_blank")
        consts_set = sem("consts_set")
        k_hi_done = sem("k_hi_done")
        k_lo_done = sem("k_lo_done")
        k_spread = [sem("k_spread0"), sem("k_spread1")]
        pair_turned = sem("pair_turned")
        pair_done = sem("pair_done")
        pair_hi_done = sem("pair_hi_done")
        pair_lo_done = sem("pair_lo_done")
        mov_hi_done = sem("mov_hi_done")
        mov_lo_done = sem("mov_lo_done")
        tile_done = sem("tile_done")
        prod_done = sem("prod_done")
        summed = sem("summed")
        z_done = sem("z_done")
        h1_ps_done = sem("h1_ps_done")
        h1_done = sem("h1_done")
        h2_ps_done = sem("h2_ps_done")
        h2_done = sem("h2_done")
        y_ps_done = sem("y_ps_done")
        y_done = sem("y_done")
        stored = sem("stored")

        block = ctx.enter_context(nc.Block())

        @block.sync
        def _(sp):
            def load_chunk(k):
                sp.dma_start(k_raw[:, k % RAW_SLOTS, :],
                             kmat[:, k * CHUNK_COLS:(k + 1) * CHUNK_COLS]).then_inc(raw_loaded[k % RAW_SLOTS], 16)

            def spread_chunk(k):
                sp.wait_ge(k_lo_done, k + 1)
                if k >= K_SLOTS:
                    sp.wait_ge(tile_done, CHUNK_LAST[k - OWN_SLOTS] + 1)
                for part, (to, split) in enumerate([(slice(0, 64), k_hi), (slice(64, 128), k_lo)] * 2):
                    n = part // 2
                    sp.dma_start(k_slot(k)[to, CHUNK_COLS * n:CHUNK_COLS * (n + 1)].bitcast(f32),
                                 split[64 * n:64 * n + 64, k % 2, :].bitcast(f32)).then_inc(k_spread[k % 2], 16)

            sp.dma_start(idx[:, :], ids).then_inc(idx_loaded, 16)
            for k in range(RAW_SLOTS):
                load_chunk(k)
            for dst, src in ((w3_sb[:, :], w3), (b1_sb[:, :], b1), (b2_sb[:, :], b2)):
                sp.dma_start(dst, src).then_inc(small_loaded, 16)
            for step in ORDER:
                if step[0] == "spread":
                    spread_chunk(step[1])
                    if step[1] + RAW_SLOTS < CHUNKS:
                        load_chunk(step[1] + RAW_SLOTS)
                if step[0] == "read":
                    bank, h = step[1:]
                    sp.wait_ge(z_done, NUMBER[step])
                    for n, tile in enumerate(CTX_TILES):
                        if tile // BANK_TILES == bank:
                            row = 32 * (tile % GROUP) + 2 * (tile % BANK_TILES // GROUP) + 1
                            sp.dma_start(z_bank(bank, h)[row:row + 1, :], ctx_t[n:n + 1, spans((h,))]).then_inc(
                                last_ctx_loaded if bank == BANKS - 1 else ctx_loaded, 16)
                if step == ("spread", CHUNKS - 1):
                    sp.wait_ge(k_lo_done, CHUNKS)
                    sp.dma_start(w1_sb, w1.rearrange("(k p) f -> p k f", p=P)).then_inc(w1_loaded, 16)
                if step == ("pair", PAIR_OF[-1]):
                    sp.wait_ge(pair_turned, NUMBER[step])
                    sp.dma_start(w2_sb, w2.rearrange("(k p) f -> p k f", p=P)).then_inc(w2_loaded, 16)
            sp.wait_ge(y_done, HALVES)
            sp.dma_start(out.rearrange("b one -> one b"), y_sb).then_inc(stored, 16)
            sp.wait_ge(stored, 16)

        @block.gpsimd
        def _(pool):
            def gather(load):
                f, halves = LOADS[load]
                for old in ROW_TAKES[load // 2]:
                    pool.wait_ge(pair_turned, old + 1)
                for n, t in enumerate(range(halves[0] * HT, (halves[-1] + 1) * HT)):
                    nc.gpsimd.indirect_dma_start(
                        out=rows[:, ROW_AT[load // 2] * HT + n, load % 2, :], out_offset=None, in_=tables[f],
                        in_offset=bass.IndirectOffsetOnAxis(ap=idx[:, f * BT + t:f * BT + t + 1], axis=0),
                    ).then_inc(rows_loaded[load % (2 * ROW_SLOTS)], 16)

            pool.wait_ge(idx_loaded, 16)
            gather(0)
            gather(1)
            nc.gpsimd.memset(ident[:, :], 0.0).then_inc(ident_blank, 1)
            pool.wait_ge(ident_blank, 1)
            nc.gpsimd.affine_select(out=ident[:, :], in_=ident[:, :], compare_op=ALU.not_equal, fill=1.0, base=0,
                                    pattern=[[-1, P]], channel_multiplier=1).then_inc(consts_set, 1)
            for load in range(2, len(LOADS)):
                gather(load)

        @block.tensor
        def _(pe):
            def wait_slot(step):
                for old in PSUM_TAKES[step]:
                    pe.wait_ge(prod_done if old[0] == "tile" else pair_done, NUMBER[old])

            def transpose_pair(step):
                load, halves = LOAD_OF[step[1]] // 2 * 2, STEPS[step[1]][1]
                for n in (load, load + 1):
                    pe.wait_ge(rows_loaded[n % (2 * ROW_SLOTS)], rows_count(n))
                wait_slot(step)
                width = HB * len(halves)
                for n in range(HT * len(halves)):
                    two_fields = rows[:, ROW_AT[load // 2] * HT + n, :, :].rearrange("p f j -> p (f j)")
                    last = nc.tensor.transpose(slot(step, width)[:, n * P:(n + 1) * P], two_fields, ident[:, :])
                last.then_inc(pair_turned, 1)

            def make_tile(step):
                u = step[1]
                s, parts = UNITS[u]
                if u == FIRST_UNIT[s]:
                    pe.wait_ge(mov_hi_done, 2 * (s + 1))
                    pe.wait_ge(mov_lo_done, 2 * (s + 1))
                for k in sorted({tile // CHUNK for tile, _ in parts}):
                    if u == CHUNK_FIRST[k]:
                        pe.wait_ge(k_spread[k % 2], 64 * (k // 2 + 1))
                wait_slot(step)
                for n, (tile, h) in enumerate(parts):
                    k_tile = k_slot(tile // CHUNK)[:, tile % CHUNK * P:(tile % CHUNK + 1) * P]
                    bank = psum[:, PSUM_AT[step] + n, :]
                    field = MOV_AT[s] + STEPS[s][1].index(h)
                    b = slice(field * HB, (field + 1) * HB)
                    nc.tensor.matmul(bank, k_tile, mov_hi[:, b], start=True, stop=False)
                    last = nc.tensor.matmul(bank, k_tile, mov_lo[:, b], start=False, stop=True)
                last.then_inc(tile_done, 1)

            def sum_group(step):
                group, h = step[1:]
                t = group % BANK_GROUPS
                if t == 0 and group:
                    pe.wait_ge(z_done, NUMBER["read", group // BANK_GROUPS - 1, h])
                pe.wait_ge(prod_done, UNIT_OF[GROUP * group + GROUP - 1, h] + 1)
                for g in range(GROUP):
                    part = (GROUP * group + g, h)
                    place = PROD_AT[UNIT_OF[part]] + UNITS[UNIT_OF[part]][1].index(part)
                    last = nc.tensor.matmul(z_ps[32 * g:32 * g + 32, h, :], pick[:, 30 - 2 * t:62 - 2 * t],
                                            prod[:, place * HB:(place + 1) * HB],
                                            start=t == 0, stop=t == BANK_GROUPS - 1)
                last.then_inc(summed, 1)

            pe.wait_ge(consts_set, 3)
            for step in ORDER:
                if step[0] == "pair":
                    transpose_pair(step)
                if step[0] == "tile":
                    make_tile(step)
                if step[0] == "sum":
                    sum_group(step)

            def layer1(half, m, k):
                return nc.tensor.matmul(psum[:, 4 * half + m, :], w1_sb[:, k, m * P:(m + 1) * P],
                                        z_bank(k, half), start=k == 0, stop=k == BANKS - 1)

            pe.wait_ge(w1_loaded, 16)
            pe.wait_ge(prod_done, len(UNITS))
            pe.wait_ge(ctx_loaded, 16 * HALVES * sum(t // BANK_TILES < BANKS - 1 for t in CTX_TILES))
            for m in range(H1 // P):
                for k in range(BANKS - 1):
                    layer1(0, m, k)
            pe.wait_ge(last_ctx_loaded, 16 * HALVES * sum(t // BANK_TILES == BANKS - 1 for t in CTX_TILES))
            for m in range(H1 // P):
                layer1(0, m, BANKS - 1).then_inc(h1_ps_done, 1)
            for m in range(H1 // P):
                for k in range(BANKS):
                    last = layer1(1, m, k)
                last.then_inc(h1_ps_done, 1)
            pe.wait_ge(w2_loaded, 16)
            pe.wait_ge(small_loaded, 3 * 16)
            for half in range(HALVES):
                pe.wait_ge(h1_done, H1 // P * (half + 1))
                for m in range(H2 // P):
                    for k in range(H1 // P):
                        last = nc.tensor.matmul(psum[:, 4 * half + m, :], w2_sb[:, k, m * P:(m + 1) * P],
                                                h1[:, k, spans((half,))], start=k == 0, stop=k == H1 // P - 1)
                    last.then_inc(h2_ps_done, 1)
            pe.wait_ge(h2_done, HALVES * H2 // P)
            for k in range(H2 // P):
                for half in range(HALVES):
                    last = nc.tensor.matmul(psum[32 * half:32 * half + 1, 4 * half + 2, :], w3_sb[:, k:k + 1],
                                            h2[:, k, spans((half,))], start=k == 0, stop=k == H2 // P - 1)
                    if k == H2 // P - 1:
                        last.then_inc(y_ps_done, 1)

        @block.scalar
        def _(act):
            def round_chunk(k):
                act.wait_ge(raw_loaded[k % RAW_SLOTS], 16 * (k // RAW_SLOTS + 1))
                if k >= 2:
                    act.wait_ge(k_spread[k % 2], 64 * (k // 2))
                nc.scalar.copy(k_hi[:, k % 2, :], k_raw[:, k % RAW_SLOTS, :]).then_inc(k_hi_done, 1)

            def keep_pair(step):
                c, halves = STEPS[step[1]]
                act.wait_ge(pair_turned, NUMBER[step])
                if c // 2 in LATE_PAIRS:
                    act.wait_ge(tile_done, CHUNK_LAST[LATE_PAIRS.index(c // 2)] + 1)
                nc.scalar.copy(pair(c // 2, halves), slot(step, HB * len(halves))).then_inc(pair_done, 1)

            def round_pair(s):
                c, halves = STEPS[s]
                act.wait_ge(pair_done, NUMBER["pair", s])
                if s:
                    act.wait_ge(mov_lo_done, 2 * s)
                nc.scalar.copy(pair_lo[:, 0:HB * len(halves)].bitcast(f32r),
                               pair(c // 2, halves)).then_inc(pair_hi_done, 1)

            def round_field(s):
                c, halves = STEPS[s]
                act.wait_ge(pair_done, NUMBER["pair", PAIR_OF[s]])
                if MOV_TAKES[s]:
                    act.wait_ge(tile_done, FIRST_UNIT[MOV_TAKES[s][-1] + 1])
                b = slice(MOV_AT[s] * HB, MOV_AT[s] * HB + HB * len(halves))
                for half in (slice(0, 64), slice(64, 128)):
                    nc.scalar.copy(mov_hi[half, b], pair(c // 2, halves)[own(c), :]).then_inc(mov_hi_done, 1)

            def copy_lo(s):
                c, halves = STEPS[s]
                act.wait_ge(pair_lo_done, NUMBER["pair", PAIR_OF[s]])
                width = HB * len(halves)
                b = slice(MOV_AT[s] * HB, MOV_AT[s] * HB + width)
                for half in (slice(0, 64), slice(64, 128)):
                    nc.scalar.copy(mov_lo[half, b], pair_lo[own(c), 0:width]).then_inc(mov_lo_done, 1)

            def read_bank(step):
                bank, h = step[1:]
                act.wait_ge(summed, NUMBER["sum", BANK_GROUPS * (bank + 1) - 1, h])
                nc.scalar.copy(z_bank(bank, h), z_ps[:, h, :]).then_inc(z_done, 1)

            for step in ORDER:
                if step[0] == "round":
                    round_chunk(step[1])
                if step[0] == "pair":
                    keep_pair(step)
                if step[0] == "lo":
                    round_pair(step[1])
                if step[0] == "field":
                    round_field(step[1])
                if step[0] == "copy":
                    copy_lo(step[1])
                if step[0] == "read":
                    read_bank(step)

            act.wait_ge(small_loaded, 3 * 16)
            for half in range(HALVES):
                for m in range(H1 // P):
                    act.wait_ge(h1_ps_done, H1 // P * half + m + 1)
                    nc.scalar.activation(h1[:, m, spans((half,))], psum[:, 4 * half + m, :], ACT.Relu,
                                         bias=b1_sb[:, m:m + 1]).then_inc(h1_done, 1)
            for half in range(HALVES):
                for m in range(H2 // P):
                    act.wait_ge(h2_ps_done, H2 // P * half + m + 1)
                    nc.scalar.activation(h2[:, m, spans((half,))], psum[:, 4 * half + m, :], ACT.Relu,
                                         bias=b2_sb[:, m:m + 1]).then_inc(h2_done, 1)
            for half in range(HALVES):
                act.wait_ge(y_ps_done, half + 1)
                nc.scalar.copy(y_sb[:, spans((half,))],
                               psum[32 * half:32 * half + 1, 4 * half + 2, :]).then_inc(y_done, 1)

        @block.vector
        def _(dve):
            def finish_chunk(k):
                dve.wait_ge(k_hi_done, k + 1)
                if k >= 2:
                    dve.wait_ge(k_spread[k % 2], 64 * (k // 2))
                nc.vector.tensor_tensor(k_lo[:, k % 2, :], k_raw[:, k % RAW_SLOTS, :], k_hi[:, k % 2, :].bitcast(f32),
                                        ALU.subtract).then_inc(k_lo_done, 1)

            def finish_pair(s):
                c, halves = STEPS[s]
                dve.wait_ge(pair_hi_done, NUMBER["pair", s])
                lo = pair_lo[:, 0:HB * len(halves)]
                nc.vector.tensor_tensor(lo, pair(c // 2, halves), lo,
                                        ALU.subtract).then_inc(pair_lo_done, 1)

            def multiply(step):
                u = step[1]
                s, parts = UNITS[u]
                c, halves = STEPS[s]
                dve.wait_ge(tile_done, u + 1)
                if u == FIRST_UNIT[s]:
                    dve.wait_ge(pair_done, NUMBER["pair", PAIR_OF[s]])
                if PROD_TAKES[u]:
                    dve.wait_ge(summed, max(NUMBER["sum", tile // GROUP, h]
                                            for old in PROD_TAKES[u] for tile, h in UNITS[old][1]))
                width = HB * len(parts)
                dst = prod[:, PROD_AT[u] * HB:PROD_AT[u] * HB + width]
                src = slot(step, width)
                r = parts[0][0] - FIRST[c]
                if len(halves) == 2:
                    nc.vector.tensor_tensor(dst, src, pair(r, halves), ALU.mult).then_inc(prod_done, 1)
                else:
                    fields = early_pairs[:, r:r + len(parts), spans(halves)]
                    nc.vector.tensor_tensor(dst.rearrange("p (n b) -> p n b", b=HB),
                                            src.rearrange("p (n b) -> p n b", b=HB),
                                            fields, ALU.mult).then_inc(prod_done, 1)

            nc.vector.memset(pick[:, :], 0.0).then_inc(pick_blank, 1)
            dve.wait_ge(pick_blank, 1)
            nc.vector.memset(pick[0:64, 30:31], 1.0).then_inc(consts_set, 1)
            nc.vector.memset(pick[64:128, 31:32], 1.0).then_inc(consts_set, 1)
            for step in ORDER:
                if step[0] == "finish":
                    finish_chunk(step[1])
                if step[0] == "lo":
                    finish_pair(step[1])
                if step[0] == "tile":
                    multiply(step)


def kernel(ids, dense_ctx, W_top1, b_top1, W_top2, b_top2, W_top3, L0_rec_kernel, **tables):
    import numpy as np
    import concourse.bacc as bacc
    from concourse.bass_utils import run_bass_kernel_spmd

    slots, spare = [], []
    for c in range(1, FIELDS):
        for r in range(c + c % 2):
            if r < c:
                slots.append(r * FIELDS - r * (r + 1) // 2 + c - r - 1)
            else:
                spare.append(len(slots))
                slots.append(-1)
    kept = np.array([s for s, p in enumerate(slots) if p >= 0])
    pair = np.array([p for p in slots if p >= 0])
    K = np.asarray(L0_rec_kernel)
    kmat = np.zeros((EMBED, len(slots), EMBED), K.dtype)
    kmat[:, kept] = K[:, pair]

    tile = np.arange(len(slots)) // 2
    place = (P * (tile // BANK_TILES) + 32 * (tile % GROUP) + 2 * (tile % BANK_TILES // GROUP)
             + np.arange(len(slots)) % 2)
    W1 = np.asarray(W_top1)
    w1 = np.zeros_like(W1)
    w1[place[kept]] = W1[pair]
    w1[place[np.array(spare)]] = W1[len(pair):]

    arrays = {
        "ids": np.ascontiguousarray(np.asarray(ids).reshape(BT, P, FIELDS).transpose(1, 2, 0).reshape(P, FIELDS * BT)),
        "kmat": np.ascontiguousarray(kmat.reshape(EMBED, CHUNKS, 2, CHUNK_COLS).transpose(2, 0, 1, 3).reshape(P, -1)),
        "ctx_t": np.ascontiguousarray(np.asarray(dense_ctx).T),
        "w1": w1,
        "b1": np.ascontiguousarray(np.asarray(b_top1).reshape(-1, P).T),
        "w2": np.ascontiguousarray(np.asarray(W_top2)),
        "b2": np.ascontiguousarray(np.asarray(b_top2).reshape(-1, P).T),
        "w3": np.ascontiguousarray(np.asarray(W_top3).reshape(-1, P).T),
    }
    for f in range(FIELDS):
        arrays[f"tbl_{f}"] = np.ascontiguousarray(np.asarray(tables[f"tbl_{f}"]))

    nc = bacc.Bacc("TRN2", target_bir_lowering=False, num_devices=1)
    ap = {name: nc.dram_tensor(f"{name}_dram", a.shape, mybir.dt.from_np(a.dtype), kind="ExternalInput").ap()
          for name, a in arrays.items()}
    out = nc.dram_tensor("y_dram", (BATCH, 1), mybir.dt.float32, kind="ExternalOutput").ap()
    build(nc, ap["ids"], [ap[f"tbl_{f}"] for f in range(FIELDS)], ap["kmat"], ap["ctx_t"],
          ap["w1"], ap["b1"], ap["w2"], ap["b2"], ap["w3"], out)
    result = run_bass_kernel_spmd(nc, [{f"{name}_dram": a for name, a in arrays.items()}], core_ids=[0])
    return result.results[0]["y_dram"]
```
